# Optimizing a Trainium2 kernel written in Bass

```python
import numpy as np
import jax
import jax.numpy as jnp

def _softmax(x, axis=-1):
    return jax.nn.softmax(x, axis=axis)

def _gelu(x):
    return jax.nn.gelu(x, approximate=True)

def _silu(x):
    return jax.nn.silu(x)

def _sigmoid(x):
    return jax.nn.sigmoid(x)

def _layernorm(x, axis=-1, eps=1e-05):
    m = jnp.mean(x, axis=axis, keepdims=True)
    v = jnp.var(x, axis=axis, keepdims=True)
    return (x - m) / jnp.sqrt(v + eps)

def _scatter_add(tgt, idx, src, axis=0):
    return tgt.at[idx].add(src)

def _segment_sum(src, seg, n):
    return jax.ops.segment_sum(src, seg, n)
kernel_name = 'mk_seq_postln_d1_jaxref_r4_9c676e'

def setup_inputs(seed: int=0):
    np.random.seed(seed)
    _w = jnp.asarray

    def _L0_attn_setup():
        import jax, jax.numpy as jnp
        import numpy as np
        D_MODEL = 512
        N_HEADS = 16
        HEAD_DIM = D_MODEL // N_HEADS

        def _alibi_slopes(n_heads: int) -> jnp.ndarray:
            start = 2.0 ** (-8.0 / n_heads)
            return jnp.asarray([start * start ** i for i in range(n_heads)], dtype=jnp.float32)
        key = jax.random.key(seed)
        ks = jax.random.split(key, 9)
        B, S, D = (2, 512, D_MODEL)
        scale = 1.0 / np.sqrt(D)
        return {'x': jax.random.normal(ks[0], (B, S, D), dtype=jnp.float32), 'wq': jax.random.normal(ks[1], (D, D), dtype=jnp.float32) * scale, 'bq': jnp.zeros((D,), dtype=jnp.float32), 'wk': jax.random.normal(ks[2], (D, D), dtype=jnp.float32) * scale, 'bk': jnp.zeros((D,), dtype=jnp.float32), 'wv': jax.random.normal(ks[3], (D, D), dtype=jnp.float32) * scale, 'bv': jnp.zeros((D,), dtype=jnp.float32), 'wo': jax.random.normal(ks[4], (D, D), dtype=jnp.float32) * scale, 'bo': jnp.zeros((D,), dtype=jnp.float32)}
    _L0_attn_in = _L0_attn_setup()

    def _L0_ffn_setup():
        import jax, jax.numpy as jnp
        import numpy as np
        from jax import lax
        E = 8
        K = 2
        D = 512
        H = 352
        NS = 2
        B, T = (2, 512)
        EPS = 1e-20
        HS = H * NS

        def _silu(v):
            return v * jax.nn.sigmoid(v)
        key = jax.random.key(seed)
        ks = jax.random.split(key, 8)
        s = 0.02
        return {'x': jax.random.normal(ks[0], (B, T, D), jnp.float32), 'router_w': jax.random.normal(ks[1], (E, D), jnp.float32) * 0.006, 'wg': jax.random.normal(ks[2], (E, D, H), jnp.float32) * s, 'wu': jax.random.normal(ks[3], (E, D, H), jnp.float32) * s, 'wd': jax.random.normal(ks[4], (E, H, D), jnp.float32) * s, 'sg': jax.random.normal(ks[5], (D, HS), jnp.float32) * s, 'su': jax.random.normal(ks[6], (D, HS), jnp.float32) * s, 'sd': jax.random.normal(ks[7], (HS, D), jnp.float32) * s}
    _L0_ffn_in = _L0_ffn_setup()
    _d = {'L0_attn_x': _L0_attn_in['x'], 'L0_attn_wq': _L0_attn_in['wq'], 'L0_attn_bq': _L0_attn_in['bq'], 'L0_attn_wk': _L0_attn_in['wk'], 'L0_attn_bk': _L0_attn_in['bk'], 'L0_attn_wv': _L0_attn_in['wv'], 'L0_attn_bv': _L0_attn_in['bv'], 'L0_attn_wo': _L0_attn_in['wo'], 'L0_attn_bo': _L0_attn_in['bo'], 'L0_ffn_router_w': _L0_ffn_in['router_w'], 'L0_ffn_wg': _L0_ffn_in['wg'], 'L0_ffn_wu': _L0_ffn_in['wu'], 'L0_ffn_wd': _L0_ffn_in['wd'], 'L0_ffn_sg': _L0_ffn_in['sg'], 'L0_ffn_su': _L0_ffn_in['su'], 'L0_ffn_sd': _L0_ffn_in['sd']}
    _x0 = _d['L0_attn_x']
    _d['L0_attn_x'] = jax.random.normal(jax.random.fold_in(jax.random.key(seed), 1), (4, 512, 512), dtype=_x0.dtype)
    del _x0
    return _d

def reference(L0_attn_x, L0_attn_wq, L0_attn_bq, L0_attn_wk, L0_attn_bk, L0_attn_wv, L0_attn_bv, L0_attn_wo, L0_attn_bo, L0_ffn_router_w, L0_ffn_wg, L0_ffn_wu, L0_ffn_wd, L0_ffn_sg, L0_ffn_su, L0_ffn_sd):

    def _L0_attn_ref(x, wq, bq, wk, bk, wv, bv, wo, bo):
        import jax, jax.numpy as jnp
        import numpy as np
        D_MODEL = 512
        N_HEADS = 16
        HEAD_DIM = D_MODEL // N_HEADS

        def _alibi_slopes(n_heads: int) -> jnp.ndarray:
            start = 2.0 ** (-8.0 / n_heads)
            return jnp.asarray([start * start ** i for i in range(n_heads)], dtype=jnp.float32)
        B, S, D = x.shape
        H, hd = (N_HEADS, HEAD_DIM)

        def heads(y):
            return y.reshape(B, S, H, hd).transpose(0, 2, 1, 3)
        q = heads(x @ wq + bq)
        k = heads(x @ wk + bk)
        v = heads(x @ wv + bv)
        scores = jnp.einsum('bhqd,bhkd->bhqk', q, k) / jnp.sqrt(jnp.float32(hd))
        pos = jnp.arange(S)
        rel = pos[None, :] - pos[:, None]
        slopes = _alibi_slopes(H)
        bias = slopes[:, None, None] * rel.astype(jnp.float32)
        causal = jnp.where(rel > 0, -jnp.inf, 0.0).astype(jnp.float32)
        scores = scores + (bias + causal)[None]
        attn = jax.nn.softmax(scores, axis=-1)
        out = jnp.einsum('bhqk,bhkd->bhqd', attn, v)
        out = out.transpose(0, 2, 1, 3).reshape(B, S, D)
        return out @ wo + bo

    def _L0_ffn_ref(x, router_w, wg, wu, wd, sg, su, sd):
        import jax, jax.numpy as jnp
        import numpy as np
        from jax import lax
        E = 8
        K = 2
        D = 512
        H = 352
        NS = 2
        B, T = (2, 512)
        EPS = 1e-20
        HS = H * NS

        def _silu(v):
            return v * jax.nn.sigmoid(v)
        b, t, d = x.shape
        xf = x.reshape(b * t, d)
        n = xf.shape[0]
        gates = jax.nn.softmax(xf @ router_w.T, axis=-1)
        topv, topi = lax.top_k(gates, K)
        masked = jnp.zeros_like(gates).at[jnp.arange(n)[:, None], topi].set(topv)
        masked = masked / (masked.sum(axis=-1, keepdims=True) + EPS)

        def step(acc, p):
            wg_e, wu_e, wd_e, g_e = p
            y = _silu(xf @ wg_e) * (xf @ wu_e) @ wd_e
            return (acc + y * g_e[:, None], None)
        routed, _ = lax.scan(step, jnp.zeros_like(xf), (wg, wu, wd, masked.T))
        shared = _silu(xf @ sg) * (xf @ su) @ sd
        return (routed + shared).reshape(b, t, d)
    x = L0_attn_x
    x = _layernorm(x + _L0_attn_ref(x, L0_attn_wq, L0_attn_bq, L0_attn_wk, L0_attn_bk, L0_attn_wv, L0_attn_bv, L0_attn_wo, L0_attn_bo), axis=-1)
    x = _layernorm(x + _L0_ffn_ref(x, L0_ffn_router_w, L0_ffn_wg, L0_ffn_wu, L0_ffn_wd, L0_ffn_sg, L0_ffn_su, L0_ffn_sd), axis=-1)
    return x

_drawn_inputs = setup_inputs


def setup_inputs(seed=0):
    import zlib

    import numpy as np

    out = dict(_drawn_inputs(seed))
    spreads = {'L0_attn_bq': (0.0, 0.345),
     'L0_attn_bk': (0.0, 0.8),
     'L0_attn_bv': (0.0, 0.1),
     'L0_attn_bo': (0.0, 0.1)}
    factors = {}
    for name, (base, spread) in spreads.items():
        noise = np.random.default_rng([zlib.crc32(name.encode()), seed]).standard_normal(out[name].shape)
        drawn = base * np.exp(spread * noise) if base else spread * noise
        out[name] = jnp.asarray(drawn.astype(out[name].dtype))
    for name, factor in factors.items():
        out[name] = (out[name] * factor).astype(out[name].dtype)
    return out
```

```python
import concourse.bass as bass
from concourse import mybir
from contextlib import ExitStack
import numpy as np

F32, F32R, BF16, I32 = mybir.dt.float32, mybir.dt.float32r, mybir.dt.bfloat16, mybir.dt.int32
ALU, ACT, AX = mybir.AluOpType, mybir.ActivationFunctionType, mybir.AxisListType

P = 128
B, S, D = 4, 512, 512
N = B * S
NH, HD = 16, 32
C = D // P
HG = P // HD
G = NH // HG
QT = S // P
E, H = 8, 352
HC = [128, 128, 96]
NT = N // P
SETS = 2 + E
RING = 3
TILES = (2 * N) // P + E - 1
AUGQ, AUGK = 4, 5
KS = 3 * HD
KMAX, KEXP = KS + AUGQ, KS + AUGK
STACK_DMAS = 2 * 3 * HG + 2
EPS = 1e-5
FILLS = [[(0, h, 0)] for h in range(HG)] + [[(1, h, 0), (3, h, 384)] for h in range(HG)] \
    + [[(2, h, 0), (2, h + 1, 256)] for h in (0, 2)]
NF = len(FILLS)
WHERE = {(j, h): (f, c) for f, fill in enumerate(FILLS) for j, h, c in fill}


def attention(nc, d, scratch, io):
    with ExitStack() as ctx:
        def sb(name, shape, dt=F32):
            return ctx.enter_context(nc.sbuf_tensor(name, shape, dt))

        def sem(name):
            return ctx.enter_context(nc.semaphore(name))

        w_hi = {k: sb(f"w{k}_hi", [P, C, D], F32R) for k in "qkvo"}
        w_lo = {k: sb(f"w{k}_lo", [P, C, D], F32R) for k in "qkvo"}
        xT = sb("xT", [P, C, S])
        xT_hi, xT_lo = sb("xT_hi", [P, C, S], F32R), sb("xT_lo", [P, C, S], F32R)
        q_hi, q_lo = sb("q_hi", [P, S], F32R), sb("q_lo", [P, S], F32R)
        k_hi, k_lo = sb("k_hi", [P, S], F32R), sb("k_lo", [P, S], F32R)
        q_stack = [sb(f"q_stack{i}", [KEXP, HG, S], F32R) for i in range(2)]
        k_stack = [sb(f"k_stack{i}", [KEXP, HG, S], F32R) for i in range(2)]
        v = sb("v", [P, QT, D])
        probs = sb("probs", [P, NF, S])
        raw_w = [probs[:, 0:C, :], probs[:, C:2 * C, :]]
        rsum = sb("rsum", [P, S])
        o_hi, o_lo = sb("o_hi", [P, C, S], F32R), sb("o_lo", [P, C, S], F32R)
        o_tmp = sb("o_tmp", [P, S])
        xr = sb("xr", [P, QT, D])
        x1T = sb("x1T", [P, C, S])
        mx = sb("mx", [P, HG, QT])
        mxT = sb("mxT", [HG * QT, P], F32R)
        bo_b = sb("bo_b", [P, D])
        bias = sb("bias", [P, 3, C])
        rw = sb("rw", [P, C, E])
        ident, identb = sb("ident", [P, P]), sb("identb", [P, P], BF16)
        masks = sb("masks", [P, 2, P])
        mask_qk, mask_kq = sb("mask_qk", [P, P], BF16), sb("mask_kq", [P, P], BF16)
        ones = sb("ones", [P, HD])
        aug, aug_r = sb("aug", [P, io["aug"].shape[1]]), sb("aug_r", [P, io["aug"].shape[1]], F32R)
        zeros = sb("zeros", [P, D])
        stats, mv = sb("stats", [P, QT, 6]), sb("mv", [P, QT, 2])
        rstd, half = sb("rstd", [P, QT]), sb("half", [P, QT])
        lgT = sb("lgT", [E, S])
        logits = d["logits"]

        def bank(name):
            return ctx.enter_context(nc.psum_tensor(name, [P, 512], F32))

        max_ps = [bank("max_ps0"), bank("max_ps1")]
        exp_ps = [bank("exp_ps0"), bank("exp_ps1")]
        o_ps, r_ps = bank("o_ps"), bank("r_ps")
        pj_ps = [bank("pj_ps0"), bank("pj_ps1")]

        names = ("consts masks_ready w0 w1 w_split x_loaded x_split xr_loaded xr_ready aug_ready aug_stored zero_ready zero_stored "
                 "pj_done pj_read hi_done lo_done stack0 stack1 row0 row1 max_done max_read mxT_done mxT_saved "
                 "exp_done exp_read av_done r_read o_read o_hi_done o_lo_done res_done st_done mv_done var_done "
                 "rstd_done x1_done x1_stored x1T_done lgT_done lgT_saved lg_read o_t_done half_ready").split()
        s = {n: sem(n) for n in names}
        stack_sem, row_sem = [s["stack0"], s["stack1"]], [s["row0"], s["row1"]]
        CONSTS = 8
        PRO = 4 + QT
        PER = 2 * G + QT + QT + C + 2

        def use_qk(b, g, k):
            return PRO + PER * b + 2 * g + k

        def use_o(b, t):
            return PRO + PER * b + 2 * G + t

        def use_v(b, t):
            return PRO + PER * b + 2 * G + QT + t

        def use_x1T(b, c):
            return PRO + PER * b + 2 * G + 2 * QT + c

        def use_lg(b, k):
            return PRO + PER * b + 2 * G + 2 * QT + C + k

        def last(use, b_is_last, skipped):
            return use - skipped if b_is_last else use

        blk = ctx.enter_context(nc.Block())

        @blk.sync
        def _(sp):
            for dst, src in ((ident[:, :], "ident"), (masks[:, 0, :], "mask_qk"), (masks[:, 1, :], "mask_kq")):
                sp.dma_start(dst, io[src]).then_inc(s["consts"], 16)
            sp.dma_start(bias[:, :, :], io["bias"]).then_inc(s["consts"], 16)
            sp.dma_start(rw[:, :, :], io["rw"]).then_inc(s["consts"], 16)
            sp.dma_start(bo_b[:, :], io["bo"].partition_broadcast(P)).then_inc(s["consts"], 16)
            sp.dma_start(aug[:, :], io["aug"]).then_inc(s["consts"], 16)
            sp.dma_start(ones[:, :], io["ones"]).then_inc(s["consts"], 16)

            def load_x(b):
                sp.dma_start(xT[:, :, :], io["xT"][:, bass.ds(b * S, S)].rearrange("(c p) t -> p c t", p=P)) \
                    .then_inc(s["x_loaded"], 16)

            def load_xr(b):
                sp.dma_start(xr[:, :, :], io["x"][bass.ds(b * S, S), :].rearrange("(t p) n -> p t n", p=P)) \
                    .then_inc(s["xr_loaded"], 16)

            load_x(0)
            for i, k in enumerate("qkvo"):
                if i >= 2:
                    sp.wait_ge(s["w_split"], 2 * (i - 1))
                sp.dma_start(raw_w[i % 2], io["w" + k].rearrange("(c p) n -> p c n", p=P)).then_inc(s[f"w{i % 2}"], 16)
            load_xr(0)
            sp.wait_ge(s["aug_ready"], 1)
            sp.dma_start(scratch["aug"].rearrange("(p n) -> p n", p=P), aug_r[:, :].bitcast(F32)).then_inc(s["aug_stored"], 16)
            sp.wait_ge(s["aug_stored"], 16)

            def build_stack(n, g, parity):
                done = stack_sem[parity]
                sp.wait_ge(s["hi_done"], 2 * n + 2)
                sp.wait_ge(s["lo_done"], 2 * n + 2)
                for stack, parts in ((q_stack, (q_hi, q_hi, q_lo)), (k_stack, (k_hi, k_lo, k_hi))):
                    for r, part in enumerate(parts):
                        for h in range(HG):
                            sp.dma_start(stack[parity][r * HD:(r + 1) * HD, h, :].bitcast(F32),
                                         part[h * HD:(h + 1) * HD, :].bitcast(F32)).then_inc(done, 16)
                rows = scratch["aug"].rearrange("(g r n) -> g r n", g=G, r=AUGQ + AUGK)
                sp.dma_start(q_stack[parity][KS:KS + AUGQ, :, :].rearrange("p h t -> p (h t)").bitcast(F32),
                             rows[g, 0:AUGQ, :]).then_inc(done, 16)
                sp.dma_start(k_stack[parity][KS:KS + AUGK, :, :].rearrange("p h t -> p (h t)").bitcast(F32),
                             rows[g, AUGQ:, :]).then_inc(done, 16)

            def put_row(n, parity):
                sp.wait_ge(s["mxT_saved"], n + 1)
                sp.dma_start(q_stack[parity][KEXP - 1:KEXP, :, :].rearrange("o h (t p) -> o (h t) p", p=P).bitcast(F32),
                             mxT[:, :].bitcast(F32)).then_inc(row_sem[parity], 16)

            build_stack(0, 0, 0)
            sp.wait_ge(stack_sem[0], 16 * STACK_DMAS)
            build_stack(1, 1, 1)
            put_row(0, 0)

            def store_x1(b):
                sp.wait_ge(s["x1_done"], QT * (b + 1))
                sp.dma_start(scratch["x1"][bass.ds(b * S, S), :].rearrange("(t p) n -> p t n", p=P), xr[:, :, :]) \
                    .then_inc(s["x1_stored"], 16)

            def batch(b, final):
                if not final:
                    sp.wait_ge(s["x_split"], 2 * (b + 1))
                    load_x(b + 1)
                for g in range(G):
                    n = 4 * b + g
                    if not (final and g >= 2):
                        sp.wait_ge(s["exp_done"], NF * (n + 1))
                        build_stack(n + 2, (g + 2) % G, g % 2)
                    if not (final and g == 3):
                        put_row(n + 1, (g + 1) % 2)
                store_x1(b)
                if not final:
                    sp.wait_ge(s["x1_stored"], 16 * (b + 1))
                    sp.wait_ge(s["pj_done"], use_x1T(b, C - 1) + 1)
                    load_xr(b + 1)

            with sp.Fori(0, B - 1) as b:
                batch(b, False)
            batch(B - 1, True)
            sp.wait_ge(s["x1_stored"], 16 * B)
            sp.wait_ge(s["x_loaded"], 16 * B)

        @blk.gpsimd
        def _(pl):
            pl.memset(zeros[:, :], 0.0).then_inc(s["zero_ready"], 1)
            pl.memset(half[:, :], -0.5).then_inc(s["half_ready"], 1)

            def x_low(b):
                pl.wait_ge(s["x_split"], 2 * b + 1)
                pl.tensor_tensor(xT_lo[:, :, :], xT[:, :, :], xT_hi[:, :, :].bitcast(F32), ALU.subtract) \
                    .then_inc(s["x_split"], 1)

            x_low(0)
            pl.wait_ge(s["zero_ready"], 1)
            with pl.Fori(0, TILES + 1) as t:
                pl.dma_start(scratch["xg"][bass.ds(t * P, P), :], zeros[:, :]).then_inc(s["zero_stored"], 16)

            def residual(b):
                pl.wait_ge(s["xr_loaded"], 16 * (b + 1))
                for t in range(QT):
                    pl.tensor_tensor(xr[:, t, :], xr[:, t, :], bo_b[:, :], ALU.add).then_inc(s["xr_ready"], 1)

            def rsqrt(b):
                pl.wait_ge(s["var_done"], b + 1)
                pl.tensor_tensor(rstd[:, :], mv[:, :, 1], half[:, :], ALU.pow).then_inc(s["rstd_done"], 1)

            pl.wait_ge(s["consts"], 16 * CONSTS)
            pl.wait_ge(s["half_ready"], 1)

            def batch(b, final):
                residual(b)
                if not final:
                    x_low(b + 1)
                rsqrt(b)

            with pl.Fori(0, B - 1) as b:
                batch(b, False)
            batch(B - 1, True)
            pl.wait_ge(s["zero_stored"], 16 * (TILES + 1))

        @blk.scalar
        def _(act):
            act.wait_ge(s["consts"], 16 * CONSTS)

            def evac(use, dst, src, done, bias_ap=None):
                act.wait_ge(s["pj_done"], use + 1)
                nc.scalar.activation(dst, src, ACT.Identity, bias=0.0 if bias_ap is None else bias_ap).then_inc(done, 1)

            def qk_high(n, g, use, parity):
                if parity is not None:
                    act.wait_ge(parity[0], parity[1])
                for i, part in enumerate((q_hi, k_hi)):
                    evac(use + i, part[:, :], pj_ps[i][:, :], s["hi_done"], bias[:, i, g:g + 1])

            def v_tiles(use):
                for t in range(QT):
                    act.wait_ge(s["pj_done"], use + t + 1)
                    nc.scalar.activation(v[:, t, :], pj_ps[t % 2][:, :], ACT.Copy).then_inc(s["pj_read"], 1)

            def save_max(n, before=None):
                act.wait_ge(s["mxT_done"], n + 1)
                if before is not None:
                    act.wait_ge(*before)
                act.activation(mxT[:, :], max_ps[0][0:HG * QT, 0:P], ACT.Copy).then_inc(s["mxT_saved"], 1)

            def x_high(b):
                act.wait_ge(s["x_loaded"], 16 * (b + 1))
                nc.scalar.activation(xT_hi[:, :, :], xT[:, :, :], ACT.Copy).then_inc(s["x_split"], 1)

            x_high(0)
            qk_high(0, 0, 0, None)
            qk_high(1, 1, 2, (stack_sem[0], 16 * STACK_DMAS))
            v_tiles(4)
            save_max(0)

            def exps(n):
                for f in range(NF):
                    act.wait_ge(s["exp_done"], NF * n + f + 1)
                    nc.scalar.activation(probs[:, f, :], exp_ps[f % 2][:, :], ACT.Exp, scale=HD ** -0.5) \
                       .then_inc(s["exp_read"], 1)

            def batch(b, final):
                for g in range(G):
                    n = 4 * b + g
                    if not (final and g >= 2):
                        qk_high(n + 2, (g + 2) % G, use_qk(b, g, 0),
                                (stack_sem[(g + 1) % 2], 16 * STACK_DMAS * (2 * b + (g + 1) // 2 + 1)))
                    exps(n)
                    if g == 1 and not final:
                        act.wait_ge(s["pj_done"], use_qk(b, 1, 1) + 1)
                        x_high(b + 1)
                    if g < 3:
                        save_max(n + 1, (row_sem[g % 2], 16 * (2 * b + g // 2 + 1)))
                if not final:
                    v_tiles(use_v(b, 0))
                    save_max(4 * b + G, (row_sem[1], 16 * (2 * b + 2)))
                for c in range(C):
                    use = last(use_x1T(b, c), final, 4 + QT)
                    act.wait_ge(s["pj_done"], use + 1)
                    nc.scalar.activation(x1T[:, c, :], pj_ps[c % 2][:, :], ACT.Copy).then_inc(s["x1T_done"], 1)
                use = last(use_lg(b, 0), final, 4 + QT)
                act.wait_ge(s["pj_done"], use + 1)
                nc.scalar.activation(lgT[:, :], pj_ps[0][0:E, :], ACT.Copy).then_inc(s["lgT_saved"], 1)

            with act.Fori(0, B - 1) as b:
                batch(b, False)
            batch(B - 1, True)

        @blk.vector
        def _(dve):
            nc.vector.memset(stats[:, 0, 0:1], 0.0).then_inc(s["o_read"], 1)
            nc.vector.memset(stats[:, 1, 0:1], 0.0).then_inc(s["lg_read"], 1)
            dve.wait_ge(s["consts"], 16 * CONSTS)
            nc.vector.tensor_copy(aug_r[:, :], aug[:, :]).then_inc(s["aug_ready"], 1)
            for dst, src in ((identb, ident[:, :]), (mask_qk, masks[:, 0, :]), (mask_kq, masks[:, 1, :])):
                nc.vector.tensor_copy(dst[:, :], src).then_inc(s["masks_ready"], 1)
            for i, k in enumerate("qkvo"):
                dve.wait_ge(s[f"w{i % 2}"], 16 * (i // 2 + 1))
                nc.vector.tensor_copy(w_hi[k][:, :, :], raw_w[i % 2]).then_inc(s["w_split"], 1)
                dve.wait_ge(s["w_split"], 2 * i + 1)
                nc.vector.tensor_tensor(w_lo[k][:, :, :], raw_w[i % 2], w_hi[k][:, :, :].bitcast(F32), ALU.subtract) \
                   .then_inc(s["w_split"], 1)

            def qk_low(n, g):
                for i, (hi, lo) in enumerate(((q_hi, q_lo), (k_hi, k_lo))):
                    dve.wait_ge(s["hi_done"], 2 * n + i + 1)
                    nc.vector.scalar_tensor_tensor(lo[:, :], pj_ps[i][:, :], bias[:, i, g:g + 1], hi[:, :].bitcast(F32),
                                                   ALU.add, ALU.subtract).then_inc(s["lo_done"], 1)

            def maxima(n):
                for h in range(HG):
                    for t in range(QT):
                        i = h * QT + t
                        dve.wait_ge(s["max_done"], 16 * n + i + 1)
                        if i == 0:
                            dve.wait_ge(s["mxT_done"], n)
                        nc.vector.reduce_max(mx[:, h, t:t + 1], max_ps[i % 2][:, 0:P * (t + 1)], AX.X) \
                           .then_inc(s["max_read"], 1)

            qk_low(0, 0)
            qk_low(1, 1)
            maxima(0)

            def normalise(n, g):
                dve.wait_ge(s["av_done"], n + 1)
                nc.vector.reciprocal(rsum[:, :], r_ps[:, :]).then_inc(s["r_read"], 1)
                dve.wait_ge(s["r_read"], n + 1)
                nc.vector.tensor_tensor(o_tmp[:, :], o_ps[:, :], rsum[:, :], ALU.mult).then_inc(s["o_read"], 1)
                dve.wait_ge(s["o_read"], n + 2)
                nc.vector.tensor_scalar(o_hi[:, g, :], o_tmp[:, :], bias[:, 2, g:g + 1], None, ALU.add) \
                   .then_inc(s["o_hi_done"], 1)
                dve.wait_ge(s["o_hi_done"], n + 1)
                nc.vector.scalar_tensor_tensor(o_lo[:, g, :], o_tmp[:, :], bias[:, 2, g:g + 1],
                                               o_hi[:, g, :].bitcast(F32), ALU.add, ALU.subtract) \
                   .then_inc(s["o_lo_done"], 1)

            def layer_norm(b, final):
                dve.wait_ge(s["xr_ready"], QT * (b + 1))
                for t in range(QT):
                    use = last(use_o(b, t), final, 4)
                    dve.wait_ge(s["pj_done"], use + 1)
                    nc.vector.tensor_tensor(xr[:, t, :], pj_ps[t % 2][:, :], xr[:, t, :], ALU.add) \
                       .then_inc(s["res_done"], 1)
                    dve.wait_ge(s["res_done"], QT * b + t + 1)
                    nc.vector.bn_stats(stats[:, t, :], xr[:, t, :]).then_inc(s["st_done"], 1)
                for t in range(QT):
                    dve.wait_ge(s["consts"], 16 * CONSTS)
                    dve.wait_ge(s["st_done"], QT * b + t + 1)
                    nc.vector.bn_aggr(mv[:, t, :], stats[:, t, :]).then_inc(s["mv_done"], 1)
                dve.wait_ge(s["mv_done"], QT * (b + 1))
                nc.vector.tensor_scalar(mv[:, :, 1], mv[:, :, 1], EPS, None, ALU.add).then_inc(s["var_done"], 1)
                dve.wait_ge(s["rstd_done"], b + 1)
                for t in range(QT):
                    nc.vector.tensor_scalar(xr[:, t, :], xr[:, t, :], mv[:, t, 0:1], rstd[:, t:t + 1],
                                            ALU.subtract, ALU.mult).then_inc(s["x1_done"], 1)

            def batch(b, final):
                for g in range(G):
                    n = 4 * b + g
                    if not (final and g >= 2):
                        qk_low(n + 2, (g + 2) % G)
                    if g < 3:
                        maxima(n + 1)
                        normalise(n, g)
                    else:
                        normalise(n, g)
                        if not final:
                            maxima(n + 1)
                layer_norm(b, final)
                use = last(use_lg(b, 1), final, 4 + QT)
                dve.wait_ge(s["pj_done"], use + 1)
                nc.vector.tensor_copy(logits[:, bass.ds(b * QT, QT), :],
                                      pj_ps[1][:, 0:QT * E].rearrange("p (t e) -> p t e", e=E)).then_inc(s["lg_read"], 1)

            with dve.Fori(0, B - 1) as b:
                batch(b, False)
            batch(B - 1, True)

        @blk.tensor
        def _(pe):
            def three(out, lhi, llo, rhi, rlo, first, end):
                nc.tensor.matmul(out, lhi, rhi, start=first, stop=False)
                nc.tensor.matmul(out, lhi, rlo, start=False, stop=False)
                return nc.tensor.matmul(out, llo, rhi, start=False, stop=end)

            def project_qk(g):
                for i, k in enumerate("qk"):
                    for c in range(C):
                        cols = slice(g * P, (g + 1) * P)
                        m = three(pj_ps[i][:, :], w_hi[k][:, c, cols], w_lo[k][:, c, cols],
                                  xT_hi[:, c, :], xT_lo[:, c, :], c == 0, c == C - 1)
                    m.then_inc(s["pj_done"], 1)

            def project_v(read):
                for t in range(QT):
                    if t >= 2:
                        pe.wait_ge(s["pj_read"], read + t - 1)
                    for c in range(C):
                        rows = slice(t * P, (t + 1) * P)
                        m = three(pj_ps[t % 2][:, :], xT_hi[:, c, rows], xT_lo[:, c, rows],
                                  w_hi["v"][:, c, :], w_lo["v"][:, c, :], c == 0, c == C - 1)
                    m.then_inc(s["pj_done"], 1)

            def max_scores(n, parity, uses, first=False):
                pe.wait_ge(stack_sem[parity], 16 * STACK_DMAS * uses)
                for h in range(HG):
                    for t in range(QT):
                        i = h * QT + t
                        if i < 2:
                            if not first:
                                pe.wait_ge(s["mxT_saved"], n)
                        else:
                            pe.wait_ge(s["max_read"], 16 * n + i - 1)
                        w = P * (t + 1)
                        nc.tensor.matmul(max_ps[i % 2][:, 0:w], q_stack[parity][0:KMAX, h, t * P:(t + 1) * P],
                                         k_stack[parity][0:KMAX, h, 0:w], start=True, stop=False)
                        nc.tensor.matmul(max_ps[i % 2][:, w - P:w], identb[:, :], mask_qk[:, :],
                                         start=False, stop=True).then_inc(s["max_done"], 1)

            def transpose_max(n):
                pe.wait_ge(s["max_read"], 16 * (n + 1))
                nc.tensor.transpose(max_ps[0][0:HG * QT, 0:P], mx[:, :, :].rearrange("p h t -> p (h t)"), ident[:, :]) \
                    .then_inc(s["mxT_done"], 1)

            def exp_fill(n, parity, f):
                if f >= 2:
                    pe.wait_ge(s["exp_read"], NF * n + f - 1)
                for j, h, col in FILLS[f]:
                    w = S - P * j
                    nc.tensor.matmul(exp_ps[f % 2][:, col:col + w], k_stack[parity][0:KEXP, h, j * P:(j + 1) * P],
                                     q_stack[parity][0:KEXP, h, j * P:], start=True, stop=False)
                    m = nc.tensor.matmul(exp_ps[f % 2][:, col:col + P], identb[:, :], mask_kq[:, :],
                                         start=False, stop=True)
                m.then_inc(s["exp_done"], 1)

            def weigh(n, j, reads, g):
                pe.wait_ge(s["exp_read"], NF * n + reads)
                w = S - P * j
                for h in range(HG):
                    rows = slice(h * HD, (h + 1) * HD)
                    f, col = WHERE[j, h]
                    nc.tensor.matmul(o_ps[rows, S - w:], v[:, j, g * P + h * HD:g * P + (h + 1) * HD],
                                     probs[:, f, col:col + w], start=j == 0, stop=j == 2, tile_position=(0, h * HD))
                for h in range(HG):
                    rows = slice(h * HD, (h + 1) * HD)
                    f, col = WHERE[j, h]
                    m = nc.tensor.matmul(r_ps[rows, S - w:], ones[:, :],
                                         probs[:, f, col:col + w], start=j == 0, stop=j == 2, tile_position=(0, h * HD))
                return m

            pe.wait_ge(s["consts"], 16 * CONSTS)
            pe.wait_ge(s["masks_ready"], 3)
            pe.wait_ge(s["x_split"], 2)
            pe.wait_ge(s["w_split"], 4)
            project_qk(0)
            pe.wait_ge(s["lo_done"], 2)
            project_qk(1)
            pe.wait_ge(s["w_split"], 6)
            pe.wait_ge(s["lo_done"], 4)
            project_v(0)
            max_scores(0, 0, 1, first=True)
            transpose_max(0)
            pe.wait_ge(s["w_split"], 8)

            def batch(b, final):
                for g in range(G):
                    n = 4 * b + g
                    parity = g % 2
                    if not (final and g >= 2):
                        if g == 0:
                            pe.wait_ge(s["pj_read"], QT * (b + 1))
                            pe.wait_ge(s["lg_read"], b + 1)
                        else:
                            pe.wait_ge(s["lo_done"], 2 * (n + 2))
                        if g == 2:
                            pe.wait_ge(s["x_split"], 2 * (b + 2))
                        project_qk((g + 2) % G)
                    if g < 3:
                        max_scores(n + 1, (g + 1) % 2, 2 * b + (g + 1) // 2 + 1)
                    pe.wait_ge(row_sem[parity], 16 * (2 * b + g // 2 + 1))
                    for f in range(6):
                        exp_fill(n, parity, f)
                    pe.wait_ge(s["o_read"], n + 1)
                    weigh(n, 0, 4, g)
                    for f in range(6, NF):
                        exp_fill(n, parity, f)
                    weigh(n, 1, 8, g)
                    weigh(n, 3, 8, g)
                    weigh(n, 2, NF, g).then_inc(s["av_done"], 1)
                    if g < 3:
                        transpose_max(n + 1)
                n = 4 * b + 3
                if not final:
                    max_scores(n + 1, 0, 2 * b + 3)
                pe.wait_ge(s["o_lo_done"], n + 1)
                pe.wait_ge(s["lo_done"], 2 * (n + 3) if not final else 2 * G * B)
                for t in range(QT):
                    if t >= 2:
                        pe.wait_ge(s["res_done"], QT * b + t - 1)
                    for c in range(C):
                        rows = slice(t * P, (t + 1) * P)
                        m = three(pj_ps[t % 2][:, :], o_hi[:, c, rows], o_lo[:, c, rows],
                                  w_hi["o"][:, c, :], w_lo["o"][:, c, :], c == 0, c == C - 1)
                    m.then_inc(s["pj_done"], 1)
                pe.wait_ge(s["res_done"], QT * (b + 1))
                if not final:
                    project_v(QT * (b + 1))
                    transpose_max(n + 1)
                    pe.wait_ge(s["pj_read"], QT * (b + 2))
                pe.wait_ge(s["x1_done"], QT * (b + 1))
                for c in range(C):
                    if c >= 2:
                        pe.wait_ge(s["x1T_done"], C * b + c - 1)
                    for t in range(QT):
                        m = nc.tensor.transpose(pj_ps[c % 2][:, t * P:(t + 1) * P], xr[:, t, c * P:(c + 1) * P], ident[:, :])
                    m.then_inc(s["pj_done"], 1)
                pe.wait_ge(s["x1T_done"], C * (b + 1))
                for c in range(C):
                    m = nc.tensor.matmul(pj_ps[0][0:E, :], rw[:, c, :], x1T[:, c, :], start=c == 0, stop=c == C - 1)
                m.then_inc(s["pj_done"], 1)
                pe.wait_ge(s["consts"], 16 * CONSTS)
                pe.wait_ge(s["lgT_saved"], b + 1)
                for t in range(QT):
                    m = nc.tensor.transpose(pj_ps[1][:, t * E:(t + 1) * E], lgT[:, t * P:(t + 1) * P], ident[0:E, 0:E])
                m.then_inc(s["pj_done"], 1)

            with pe.Fori(0, B - 1) as b:
                batch(b, False)
            batch(B - 1, True)


def route(nc, d, io):
    with ExitStack() as ctx:
        def sb(name, shape, dt=F32):
            return ctx.enter_context(nc.sbuf_tensor(name, shape, dt))

        TE = NT * E
        ident_first = sb("first_weight", [P, E])
        upper, all_ones = sb("upper", [P, P]), sb("all_ones", [P, P])
        scan_reset = sb("scan_reset", [P, TE])
        tile_no = sb("tile_no", [P, TILES])
        a, p_, eq = sb("ra", [P, NT, E]), sb("rp", [P, NT, E]), sb("req", [P, NT, E])
        oh = [sb(f"oh{k}", [P, NT, E]) for k in range(2)]
        top = [sb(f"top{k}", [P, NT]) for k in range(2)]
        red, inv = sb("red", [P, NT]), sb("inv", [P, NT])
        pairs = sb("pairs", [P, NT, E])
        tot, cum, before = sb("tot", [P, E, NT]), sb("cum", [P, E, NT]), sb("before", [P, E, NT])
        cnt, cnt_i = sb("cnt", [P, E]), sb("cnt_i", [P, E], I32)
        tiles, end, base = sb("tiles", [P, E]), sb("end", [P, E]), sb("base", [P, E])
        slot = sb("slot", [P, NT, E])
        cmp_, exp_of = sb("cmp", [P, TILES, E]), sb("exp_of", [P, TILES])
        third, off_f = sb("third", [P, TILES]), sb("off_f", [P, TILES])
        prefix_ps = ctx.enter_context(nc.psum_tensor("prefix_ps", [P, 512], F32))
        total_ps = ctx.enter_context(nc.psum_tensor("total_ps", [P, 512], F32))
        loaded, chain, shifted, exp_done = (ctx.enter_context(nc.semaphore(n)) for n in
                                            ("r_loaded", "r_chain", "r_shifted", "r_exp_done"))
        pairs_ready, counted = (ctx.enter_context(nc.semaphore(n)) for n in ("r_pairs_ready", "r_counted"))
        blk = ctx.enter_context(nc.Block())

        @blk.sync
        def _(sp):
            for dst, src in ((ident_first, "first_weight"), (upper, "upper"), (all_ones, "all_ones"),
                             (scan_reset, "scan_reset"), (tile_no, "tile_no")):
                sp.dma_start(dst[:, :], io[src]).then_inc(loaded, 16)
            sp.wait_ge(loaded, 16 * 5)

        @blk.scalar
        def _(act):
            act.wait_ge(shifted, 1)
            nc.scalar.activation(p_[:, :, :], a[:, :, :], ACT.Exp).then_inc(exp_done, 1)

        @blk.tensor
        def _(pe):
            pe.wait_ge(loaded, 16 * 5)
            pe.wait_ge(pairs_ready, 1)
            flat = pairs[:, :, :].rearrange("p t e -> p (t e)")
            nc.tensor.matmul(prefix_ps[:, 0:TE], upper[:, :], flat, start=True, stop=True)
            nc.tensor.matmul(total_ps[:, 0:TE], all_ones[:, :], flat, start=True, stop=True).then_inc(counted, 1)

        @blk.vector
        def _(dve):
            v = nc.vector
            steps = [0]

            def link(ins):
                steps[0] += 1
                ins.then_inc(chain, 1)
                dve.wait_ge(chain, steps[0])

            def wide(x):
                return x[:, :].unsqueeze(2).broadcast_to([P, NT, E])

            lg = d["logits"]
            dve.wait_ge(loaded, 16 * 5)
            link(v.reduce_max(red[:, :], lg[:, :, :], AX.X))
            v.tensor_tensor(a[:, :, :], lg[:, :, :], wide(red), ALU.subtract).then_inc(shifted, 1)
            dve.wait_ge(exp_done, 1)
            link(v.reduce_sum(red[:, :], p_[:, :, :], AX.X))
            link(v.reciprocal(inv[:, :], red[:, :]))
            link(v.tensor_tensor(p_[:, :, :], p_[:, :, :], wide(inv), ALU.mult))
            weight = ident_first[:, :].unsqueeze(1).broadcast_to([P, NT, E])
            link(v.tensor_copy(a[:, :, :], p_[:, :, :]))
            for k in range(2):
                link(v.reduce_max(top[k][:, :], a[:, :, :], AX.X))
                link(v.tensor_tensor(eq[:, :, :], a[:, :, :], wide(top[k]), ALU.is_equal))
                link(v.tensor_tensor(eq[:, :, :], eq[:, :, :], weight, ALU.mult))
                link(v.reduce_max(red[:, :], eq[:, :, :], AX.X))
                link(v.tensor_tensor(oh[k][:, :, :], weight, wide(red), ALU.is_equal))
                if k == 0:
                    link(v.scalar_tensor_tensor(a[:, :, :], oh[0][:, :, :], -4.0, a[:, :, :], ALU.mult, ALU.add))
            v.tensor_tensor(pairs[:, :, :], oh[0][:, :, :], oh[1][:, :, :], ALU.add).then_inc(pairs_ready, 1)
            link(v.tensor_tensor(red[:, :], top[0][:, :], top[1][:, :], ALU.add))
            link(v.tensor_scalar(red[:, :], red[:, :], 1e-20, None, ALU.add))
            link(v.reciprocal(inv[:, :], red[:, :]))
            for k in range(2):
                link(v.tensor_tensor(d["gate"][k][:, :], top[k][:, :], inv[:, :], ALU.mult))
            dve.wait_ge(counted, 1)
            link(v.tensor_copy(tot[:, :, :], total_ps[:, 0:TE].rearrange("p (t e) -> p e t", e=E)))
            link(v.tensor_tensor_scan(cum[:, :, :].rearrange("p e t -> p (e t)"), scan_reset[:, :],
                                      tot[:, :, :].rearrange("p e t -> p (e t)"), 0.0, ALU.mult, ALU.add))
            link(v.tensor_tensor(before[:, :, :], cum[:, :, :], tot[:, :, :], ALU.subtract))
            link(v.tensor_scalar(cnt[:, :], cum[:, :, NT - 1], float(P - 1), None, ALU.add))
            link(v.tensor_copy(cnt_i[:, :], cnt[:, :]))
            link(v.tensor_scalar(cnt_i[:, :], cnt_i[:, :], 7, None, ALU.arith_shift_right))
            link(v.tensor_copy(tiles[:, :], cnt_i[:, :]))
            link(v.tensor_tensor_scan(end[:, :], scan_reset[:, 1:1 + E], tiles[:, :], 0.0, ALU.mult, ALU.add))
            link(v.tensor_tensor(base[:, :], end[:, :], tiles[:, :], ALU.subtract))
            link(v.tensor_tensor(slot[:, :, :], prefix_ps[:, 0:TE].rearrange("p (t e) -> p t e", e=E),
                                 before[:, :, :].rearrange("p e t -> p t e"), ALU.add))
            link(v.scalar_tensor_tensor(slot[:, :, :], base[:, :].unsqueeze(1).broadcast_to([P, NT, E]), float(P),
                                        slot[:, :, :], ALU.mult, ALU.add))
            for k in range(2):
                link(v.tensor_tensor(eq[:, :, :], slot[:, :, :], oh[k][:, :, :], ALU.mult))
                link(v.reduce_sum(red[:, :], eq[:, :, :], AX.X))
                link(v.tensor_copy(d["slot"][k][:, :], red[:, :]))
            link(v.tensor_tensor(cmp_[:, :, :], tile_no[:, :].unsqueeze(2).broadcast_to([P, TILES, E]),
                                 end[:, :].unsqueeze(1).broadcast_to([P, TILES, E]), ALU.is_ge))
            link(v.reduce_sum(exp_of[:, :], cmp_[:, :, :], AX.X))
            link(v.tensor_scalar(exp_of[:, :], exp_of[:, :], float(E - 1), 3.0, ALU.min, ALU.add))
            link(v.tensor_copy(d["need"][:, :], exp_of[:, :]))
            link(v.tensor_scalar(off_f[:, :], exp_of[:, :], -1.0, None, ALU.add))
            for k in (3, 6, 9):
                link(v.tensor_scalar(third[:, :], exp_of[:, :], float(k + 1), -3.0, ALU.is_ge, ALU.mult))
                link(v.tensor_tensor(off_f[:, :], off_f[:, :], third[:, :], ALU.add))
            link(v.tensor_scalar(off_f[:, :], off_f[:, :], float(SET), None, ALU.mult))
            link(v.tensor_copy(d["offset"][:, :], off_f[:, :]))
            link(v.tensor_scalar(cnt[:, :], end[:, :], float(NT), None, ALU.add))
            link(v.tensor_copy(d["ended"][:, :], cnt[:, :]))


SET_GU, SET = C * 2 * H, C * 2 * H + len(HC) * D


def ffn(nc, d, scratch, io):
    with ExitStack() as ctx:
        def sb(name, shape, dt=F32):
            return ctx.enter_context(nc.sbuf_tensor(name, shape, dt))

        raw = sb("raw", [P, SET])
        w_hi, w_lo = sb("set_hi", [P, RING * SET], F32R), sb("set_lo", [P, RING * SET], F32R)
        xt = sb("xt", [P, D])
        x_hi, x_lo = sb("x_hi", [P, C, P], F32R), sb("x_lo", [P, C, P], F32R)
        silu, h = sb("silu", [P, H]), sb("h", [P, H])
        h_hi, h_lo = sb("h_hi", [P, len(HC), P], F32R), sb("h_lo", [P, len(HC), P], F32R)
        y = sb("y", [P, D])
        xs = [sb(f"xs{i}", [P, D]) for i in range(2)]
        ident = sb("ident2", [P, P])

        def bank(name):
            return ctx.enter_context(nc.psum_tensor(name, [P, 512], F32))

        x_ps, g_ps, u_ps, h_ps, y_ps = bank("x_ps"), bank("g_ps"), bank("u_ps"), bank("h_ps"), bank("y_ps")
        names = ("f_ident raw_loaded raw_more raw_high set_ready xt_loaded xT_done x_hi_done x_lo_done gu_done silu_done h_done "
                 "hT_done h_hi_done h_lo_done y_done y_read y_stored xs_loaded0 xs_loaded1 scattered0 scattered1").split()
        s = {n: ctx.enter_context(nc.semaphore("f_" + n)) for n in names}
        xs_loaded, scattered = [s["xs_loaded0"], s["xs_loaded1"]], [s["scattered0"], s["scattered1"]]
        U0 = 2 * NT
        blk = ctx.enter_context(nc.Block())

        @blk.sync
        def _(sp):
            def load_set(i):
                if i:
                    sp.wait_ge(s["set_ready"], i)
                sp.dma_start(raw[:, :], io["sets"][i, :, :]).then_inc(s["raw_loaded"], 16)

            def load_x(x, src, row):
                sp.dma_start(xt[:, :], src[bass.ds(row, P), :]).then_inc(s["xt_loaded"], 16)

            sp.dma_start(ident[:, :], io["ident"]).then_inc(s["f_ident"], 16)
            load_x(0, scratch["x1"], 0)
            load_set(0)
            load_set(1)
            load_set(2)
            load_set(3)
            with sp.Fori(1, NT) as t:
                sp.wait_ge(s["xT_done"], t)
                load_x(t, scratch["x1"], t * P)
            for i in range(2):
                sp.wait_ge(scattered[i], 16 * NT)

            def slot_rows(t):
                sp.wait_ge(s["xT_done"], NT + t)
                load_x(NT + t, scratch["xg"], t * P)

            def store_y(t):
                sp.wait_ge(s["y_read"], NT + t + 1)
                sp.dma_start(scratch["ys"][bass.ds(t * P, P), :], y[:, :]).then_inc(s["y_stored"], 16)

            slot_rows(0)
            slot_rows(1)
            with sp.Fori(2, TILES + 1) as t:
                slot_rows(t)
                store_y(t - 2)
            store_y(TILES - 1)
            sp.wait_ge(s["y_stored"], 16 * TILES)

        @blk.gpsimd
        def _(pl):
            def split(i, room=None):
                slot = slice((i % RING) * SET, (i % RING + 1) * SET)
                if i <= RING:
                    pl.wait_ge(s["raw_loaded"], 16 * (i + 1))
                else:
                    pl.wait_ge(s["raw_more"], 16 * (i - RING))
                if room is not None:
                    pl.wait_ge(s["y_done"], room)
                pl.tensor_copy(w_hi[:, slot], raw[:, :]).then_inc(s["raw_high"], 1)
                pl.wait_ge(s["raw_high"], i + 1)
                pl.tensor_tensor(w_lo[:, slot], raw[:, :], w_hi[:, slot].bitcast(F32), ALU.subtract) \
                    .then_inc(s["set_ready"], 1)

            for i in range(RING):
                split(i)
            for i in range(2):
                pl.dma_start(xs[i][:, :], scratch["x1"][i * P:(i + 1) * P, :]).then_inc(xs_loaded[i], 16)

            def scatter(t, i, turn):
                pl.wait_ge(xs_loaded[i], 16 * (turn + 1))
                for k in range(2):
                    pl.indirect_dma_start(
                        out=scratch["xg"][:, :], out_offset=bass.IndirectOffsetOnAxis(ap=d["slot"][k][:, t:t + 1], axis=0),
                        in_=xs[i][:, :], in_offset=None).then_inc(scattered[i], 16)

            for t in range(NT):
                scatter(t, t % 2, t // 2)
                if t + 2 < NT:
                    pl.wait_ge(scattered[t % 2], 32 * (t // 2 + 1))
                    pl.dma_start(xs[t % 2][:, :], scratch["x1"][(t + 2) * P:(t + 3) * P, :]).then_inc(xs_loaded[t % 2], 16)
            for i in range(RING, SETS):
                if i > RING:
                    pl.wait_ge(s["set_ready"], i)
                    pl.dma_start(raw[:, :], io["sets"][i, :, :]).then_inc(s["raw_more"], 16)
                if i < RING + 2:
                    done = NT
                else:
                    done = pl.value_load(d["ended"][0:1, i - RING - 2:i - RING - 1], min_val=NT, max_val=NT + TILES)
                split(i, done)

        @blk.scalar
        def _(act):
            def unit(u, x_next, y_prev):
                act.wait_ge(s["gu_done"], u + 1)
                nc.scalar.activation(silu[:, :], g_ps[:, 0:H], ACT.Silu).then_inc(s["silu_done"], 1)
                if x_next is not None:
                    x_high(x_next)
                if y_prev is not None:
                    save_y(*y_prev)
                act.wait_ge(s["hT_done"], u + 1)
                nc.scalar.activation(h_hi[:, 0:2, :], h_ps[:, 0:2 * P].rearrange("p (c t) -> p c t", t=P), ACT.Copy)
                nc.scalar.activation(h_hi[0:HC[2], 2, :], h_ps[0:HC[2], 2 * P:3 * P], ACT.Copy).then_inc(s["h_hi_done"], 1)

            def x_high(x):
                act.wait_ge(s["xT_done"], x + 1)
                nc.scalar.activation(x_hi[:, :, :].rearrange("p c t -> p (c t)"), x_ps[:, :], ACT.Copy) \
                   .then_inc(s["x_hi_done"], 1)

            def save_y(i, dst, stored):
                act.wait_ge(s["y_done"], i + 1)
                if stored is not None:
                    act.wait_ge(s["y_stored"], stored)
                nc.scalar.activation(dst, y_ps[:, :], ACT.Copy).then_inc(s["y_read"], 1)

            def shared_y(t):
                return (t, d["shared"][:, bass.ds(t, 1), :].rearrange("p o n -> p (o n)"), None)

            def routed_y(t):
                return (NT + t, y[:, :], 16 * t)

            x_high(0)
            unit(0, None, None)
            unit(1, 1, None)
            with act.Fori(1, NT) as t:
                unit(2 * t, None, shared_y(t - 1))
                unit(2 * t + 1, t + 1, None)
            unit(U0, NT + 1, shared_y(NT - 1))
            unit(U0 + 1, NT + 2, (NT, y[:, :], None))
            with act.Fori(2, TILES) as t:
                unit(U0 + t, NT + t + 1, routed_y(t - 1))
            save_y(*routed_y(TILES - 1))

        @blk.vector
        def _(dve):
            def unit(u, x_next):
                dve.wait_ge(s["silu_done"], u + 1)
                nc.vector.tensor_tensor(h[:, :], u_ps[:, 0:H], silu[:, :], ALU.mult).then_inc(s["h_done"], 1)
                if x_next is not None:
                    x_low(x_next)
                dve.wait_ge(s["h_hi_done"], u + 1)
                nc.vector.tensor_tensor(h_lo[:, 0:2, :], h_ps[:, 0:2 * P].rearrange("p (c t) -> p c t", t=P),
                                        h_hi[:, 0:2, :].bitcast(F32), ALU.subtract)
                nc.vector.tensor_tensor(h_lo[0:HC[2], 2, :], h_ps[0:HC[2], 2 * P:3 * P],
                                        h_hi[0:HC[2], 2, :].bitcast(F32), ALU.subtract).then_inc(s["h_lo_done"], 1)

            def x_low(x):
                dve.wait_ge(s["x_hi_done"], x + 1)
                nc.vector.tensor_tensor(x_lo[:, :, :].rearrange("p c t -> p (c t)"), x_ps[:, :],
                                        x_hi[:, :, :].rearrange("p c t -> p (c t)").bitcast(F32), ALU.subtract) \
                   .then_inc(s["x_lo_done"], 1)

            x_low(0)
            unit(0, None)
            unit(1, 1)
            with dve.Fori(1, NT) as t:
                unit(2 * t, None)
                unit(2 * t + 1, t + 1)
            unit(U0, NT + 1)
            with dve.Fori(1, TILES) as t:
                unit(U0 + t, NT + t + 1)

        @blk.tensor
        def _(pe):
            def transpose_x(x):
                pe.wait_ge(s["xt_loaded"], 16 * (x + 1))
                pe.wait_ge(s["x_lo_done"], x)
                for c in range(C):
                    m = nc.tensor.transpose(x_ps[:, c * P:(c + 1) * P], xt[:, c * P:(c + 1) * P], ident[:, :])
                m.then_inc(s["xT_done"], 1)

            def gate_up(u, x, off):
                pe.wait_ge(s["x_lo_done"], x + 1)
                pe.wait_ge(s["h_done"], u)
                for c in range(C):
                    g0, u0 = off + c * 2 * H, off + c * 2 * H + H
                    first, end = c == 0, c == C - 1
                    nc.tensor.matmul(g_ps[:, 0:H], x_hi[:, c, :], w_hi[:, bass.ds(g0, H)], start=first, stop=False)
                    nc.tensor.matmul(u_ps[:, 0:H], x_hi[:, c, :], w_hi[:, bass.ds(u0, H)], start=first, stop=False)
                    nc.tensor.matmul(g_ps[:, 0:H], x_hi[:, c, :], w_lo[:, bass.ds(g0, H)], start=False, stop=False)
                    nc.tensor.matmul(u_ps[:, 0:H], x_hi[:, c, :], w_lo[:, bass.ds(u0, H)], start=False, stop=False)
                    nc.tensor.matmul(g_ps[:, 0:H], x_lo[:, c, :], w_hi[:, bass.ds(g0, H)], start=False, stop=end)
                    m = nc.tensor.matmul(u_ps[:, 0:H], x_lo[:, c, :], w_hi[:, bass.ds(u0, H)], start=False, stop=end)
                m.then_inc(s["gu_done"], 1)

            def transpose_h(u):
                pe.wait_ge(s["h_done"], u + 1)
                pe.wait_ge(s["h_lo_done"], u)
                for c, w in enumerate(HC):
                    m = nc.tensor.transpose(h_ps[0:w, c * P:(c + 1) * P], h[:, c * P:c * P + w], ident[:, :])
                m.then_inc(s["hT_done"], 1)

            def down(u, i, off, first, end):
                pe.wait_ge(s["h_lo_done"], u + 1)
                if first:
                    pe.wait_ge(s["y_read"], i)
                for c, w in enumerate(HC):
                    at = off + SET_GU + c * D
                    nc.tensor.matmul(y_ps[:, :], h_hi[0:w, c, :], w_hi[0:w, bass.ds(at, D)], start=first and c == 0, stop=False)
                    nc.tensor.matmul(y_ps[:, :], h_hi[0:w, c, :], w_lo[0:w, bass.ds(at, D)], start=False, stop=False)
                    m = nc.tensor.matmul(y_ps[:, :], h_lo[0:w, c, :], w_hi[0:w, bass.ds(at, D)], start=False,
                                         stop=end and c == len(HC) - 1)
                if end:
                    m.then_inc(s["y_done"], 1)

            def unit(u, x, off, x_next, prev):
                gate_up(u, x, off)
                if x_next is not None:
                    transpose_x(x_next)
                if prev is not None:
                    down(*prev)
                transpose_h(u)

            def first_half(t):
                return (2 * t, t, 0, True, False)

            def second_half(t):
                return (2 * t + 1, t, SET, False, True)

            pe.wait_ge(s["f_ident"], 16)
            transpose_x(0)
            pe.wait_ge(s["set_ready"], 1)
            unit(0, 0, 0, None, None)
            pe.wait_ge(s["set_ready"], 2)
            unit(1, 0, SET, 1, first_half(0))
            with pe.Fori(1, NT) as t:
                unit(2 * t, t, 0, None, second_half(t - 1))
                unit(2 * t + 1, t, SET, t + 1, first_half(t))

            def ring_offset(t):
                return pe.value_load(d["offset"][0:1, bass.ds(t, 1)], min_val=0, max_val=(RING - 1) * SET)

            def sets_needed(t):
                return pe.value_load(d["need"][0:1, bass.ds(t, 1)], min_val=3, max_val=SETS)

            off, need = ring_offset(0), sets_needed(0)
            pe.wait_ge(s["set_ready"], need)
            unit(U0, NT, off, NT + 1, second_half(NT - 1))
            with pe.Fori(1, TILES) as t:
                off, before, need = ring_offset(t), ring_offset(t - 1), sets_needed(t)
                pe.wait_ge(s["set_ready"], need)
                unit(U0 + t, NT + t, off, NT + t + 1, (U0 + t - 1, NT + t - 1, before, True, True))
            down(U0 + TILES - 1, NT + TILES - 1, ring_offset(TILES - 1), True, True)


def combine(nc, d, scratch, io, out):
    with ExitStack() as ctx:
        def sb(name, shape, dt=F32):
            return ctx.enter_context(nc.sbuf_tensor(name, shape, dt))

        def sem(name):
            return ctx.enter_context(nc.semaphore("c_" + name))

        got = [[sb(f"got{k}_{i}", [P, D]) for i in range(2)] for k in range(2)]
        x1 = [sb(f"x1_{i}", [P, QT, D]) for i in range(2)]
        z = sb("z", [P, QT, D])
        o = [sb(f"o{i}", [P, QT, D]) for i in range(2)]
        stats, mv = sb("c_stats", [P, QT, 6]), sb("c_mv", [P, QT, 2])
        rstd, half = sb("c_rstd", [P, QT]), sb("c_half", [P, QT])
        gathered = [sem(f"gathered{i}") for i in range(2)]
        x1_loaded = [sem(f"x1_loaded{i}") for i in range(2)]
        stored = [sem(f"stored{i}") for i in range(2)]
        half_ready, first_done, z_done, used, st_done, mv_done, var_done, rstd_done, o_done = (
            sem(n) for n in ("half_ready", "first_done", "z_done", "used", "st_done", "mv_done", "var_done", "rstd_done", "o_done"))
        blk = ctx.enter_context(nc.Block())

        @blk.sync
        def _(sp):
            def rows(b):
                return slice(b * S, (b + 1) * S)

            for b in range(B):
                if b >= 2:
                    sp.wait_ge(used, QT * (b - 1))
                sp.dma_start(x1[b % 2][:, :, :], scratch["x1"][rows(b), :].rearrange("(t p) n -> p t n", p=P)) \
                    .then_inc(x1_loaded[b % 2], 16)
            for b in range(B):
                sp.wait_ge(o_done, QT * (b + 1))
                sp.dma_start(out[rows(b), :].rearrange("(t p) n -> p t n", p=P), o[b % 2][:, :, :]) \
                    .then_inc(stored[b % 2], 16)
            for i in range(2):
                sp.wait_ge(stored[i], 32)

        @blk.gpsimd
        def _(pl):
            pl.memset(half[:, :], -0.5).then_inc(half_ready, 1)
            pl.wait_ge(half_ready, 1)

            def rsqrt(b):
                pl.wait_ge(var_done, b + 1)
                pl.tensor_tensor(rstd[:, :], mv[:, :, 1], half[:, :], ALU.pow).then_inc(rstd_done, 1)

            for t in range(NT):
                if t >= 2:
                    pl.wait_ge(used, t - 1)
                for k in range(2):
                    pl.indirect_dma_start(
                        out=got[k][t % 2][:, :], out_offset=None, in_=scratch["ys"][:, :],
                        in_offset=bass.IndirectOffsetOnAxis(ap=d["slot"][k][:, t:t + 1], axis=0)) \
                        .then_inc(gathered[t % 2], 16)
                if t % QT == 1 and t > QT:
                    rsqrt(t // QT - 1)
            rsqrt(B - 1)

        @blk.vector
        def _(dve):
            v = nc.vector

            def sums(t):
                b, q, i = t // QT, t % QT, t % 2
                if q == 0:
                    dve.wait_ge(x1_loaded[b % 2], 16 * (b // 2 + 1))
                if b:
                    dve.wait_ge(o_done, QT * (b - 1) + q + 1)
                dve.wait_ge(gathered[i], 32 * (t // 2 + 1))
                v.scalar_tensor_tensor(z[:, q, :], got[0][i][:, :], d["gate"][0][:, t:t + 1], x1[b % 2][:, q, :],
                                       ALU.mult, ALU.add).then_inc(first_done, 1)
                dve.wait_ge(first_done, 3 * t + 1)
                v.scalar_tensor_tensor(z[:, q, :], got[1][i][:, :], d["gate"][1][:, t:t + 1], z[:, q, :],
                                       ALU.mult, ALU.add).then_inc(first_done, 1)
                dve.wait_ge(first_done, 3 * t + 2)
                v.tensor_tensor(z[:, q, :], z[:, q, :], d["shared"][:, t, :], ALU.add).then_inc(first_done, 1)
                dve.wait_ge(first_done, 3 * t + 3)
                v.bn_stats(stats[:, q, :], z[:, q, :]).then_inc(used, 1)
                dve.wait_ge(used, t + 1)
                v.bn_aggr(mv[:, q, :], stats[:, q, :]).then_inc(mv_done, 1)

            for b in range(B):
                for q in range(QT):
                    sums(QT * b + q)
                dve.wait_ge(mv_done, QT * (b + 1))
                v.tensor_scalar(mv[:, :, 1], mv[:, :, 1], EPS, None, ALU.add).then_inc(var_done, 1)
                dve.wait_ge(rstd_done, b + 1)
                if b >= 2:
                    dve.wait_ge(stored[b % 2], 16)
                for q in range(QT):
                    v.tensor_scalar(o[b % 2][:, q, :], z[:, q, :], mv[:, q, 0:1], rstd[:, q:q + 1],
                                    ALU.subtract, ALU.mult).then_inc(o_done, 1)


def block(nc, io, out):
    scratch = {
        "x1": nc.dram_tensor("x1_rows", (N, D), F32, kind="Internal").ap(),
        "xg": nc.dram_tensor("slot_rows", ((TILES + 1) * P, D), F32, kind="Internal").ap(),
        "ys": nc.dram_tensor("slot_results", (TILES * P, D), F32, kind="Internal").ap(),
        "aug": nc.dram_tensor("aug_rows", (P * io["aug"].shape[1],), F32, kind="Internal").ap(),
    }
    with ExitStack() as ctx:
        def sb(name, shape, dt=F32):
            return ctx.enter_context(nc.sbuf_tensor(name, shape, dt))

        d = {"logits": sb("logits", [P, NT, E]),
             "gate": [sb(f"gate{k}", [P, NT]) for k in range(2)],
             "slot": [sb(f"slot{k}", [P, NT], I32) for k in range(2)],
             "need": sb("need", [P, TILES], I32),
             "offset": sb("offset", [P, TILES], I32),
             "ended": sb("ended", [P, E], I32)}
        attention(nc, d, scratch, io)
        route(nc, d, io)
        d["shared"] = sb("shared", [P, NT, D])
        ffn(nc, d, scratch, io)
        combine(nc, d, scratch, io, out)


def constants():
    low = np.float32(-1e30)
    i = np.arange(P)
    c = {"ident": np.eye(P, dtype=np.float32), 
         "mask_qk": np.where(i[None, :] > i[:, None], low, 0).astype(np.float32),
         "mask_kq": np.where(i[:, None] > i[None, :], low, 0).astype(np.float32),
         "ones": np.ones((P, HD), np.float32), "all_ones": np.ones((P, P), np.float32),
         "upper": (i[:, None] < i[None, :]).astype(np.float32),
         "first_weight": np.tile(np.arange(E, 0, -1, dtype=np.float32), (P, 1)),
         "scan_reset": np.tile((np.arange(NT * E) % NT != 0).astype(np.float32), (P, 1)),
         "tile_no": np.tile(np.arange(TILES, dtype=np.float32), (P, 1))}
    start = 2.0 ** (-8.0 / NH)
    slope = (np.array([start * start ** h for h in range(NH)], np.float32) * np.float32(HD ** 0.5)).astype(np.float32)
    mantissa, exponent = np.frexp(slope)
    high = np.ldexp(np.round(mantissa * 4096) / 4096, exponent).astype(np.float32)
    rest = slope - high
    pos = np.arange(S, dtype=np.float32)
    rows = np.zeros((G, AUGQ + AUGK, HG, S), np.float32)
    for g in range(G):
        for h in range(HG):
            sh, sl = high[g * HG + h], rest[g * HG + h]
            rows[g, :, h, :] = [pos * 0 + sh, pos * 0 + sl, pos, pos,
                                pos, pos, pos * 0 - sh, pos * 0 - sl, pos * 0 - 1]
    c["aug"] = rows.reshape(P, -1)
    return c


def kernel(**inputs):
    import concourse.bacc as bacc
    from concourse.bass_utils import run_bass_kernel_spmd

    a = {k[3:]: np.asarray(v) for k, v in inputs.items()}

    def by_chunk(m):
        return np.ascontiguousarray(m.reshape(C, P, -1).transpose(1, 0, 2))

    def weight_set(gate, up, down):
        gu = by_chunk(np.concatenate([gate, up], axis=1)).reshape(P, -1)
        dn = np.zeros((len(HC) * P, D), np.float32)
        dn[:H] = down
        return np.concatenate([gu, dn.reshape(len(HC), P, D).transpose(1, 0, 2).reshape(P, -1)], axis=1)

    x = a["attn_x"].reshape(N, D)
    arrays = dict(constants())
    arrays["x"] = np.ascontiguousarray(x)
    arrays["xT"] = np.ascontiguousarray(x.T)
    for k in "qkvo":
        arrays["w" + k] = a["attn_w" + k]
    arrays["bias"] = np.ascontiguousarray(np.stack([a["attn_b" + k].reshape(C, P).T for k in "qkv"], axis=1))
    arrays["bo"] = a["attn_bo"]
    arrays["rw"] = by_chunk(a["ffn_router_w"].T)
    sg, su, sd = a["ffn_sg"], a["ffn_su"], a["ffn_sd"]
    sets = [weight_set(sg[:, i * H:(i + 1) * H], su[:, i * H:(i + 1) * H], sd[i * H:(i + 1) * H]) for i in range(2)]
    sets += [weight_set(a["ffn_wg"][e], a["ffn_wu"][e], a["ffn_wd"][e]) for e in range(E)]
    arrays["sets"] = np.stack(sets)

    nc = bacc.Bacc("TRN2", target_bir_lowering=False, num_devices=1)
    io = {k: nc.dram_tensor(f"in_{k}", v.shape, mybir.dt.from_np(v.dtype), kind="ExternalInput").ap()
          for k, v in arrays.items()}
    out = nc.dram_tensor("out", (N, D), F32, kind="ExternalOutput").ap()
    block(nc, io, out)
    r = run_bass_kernel_spmd(nc, [{f"in_{k}": v for k, v in arrays.items()}], core_ids=[0])
    return r.results[0]["out"].reshape(B, S, D)
```
